# Optimizing a Trainium2 kernel written in Bass

```python
import numpy as np
import jax
import jax.numpy as jnp

def _softmax(x, axis=-1):
    return jax.nn.softmax(x, axis=axis)

def _gelu(x):
    return jax.nn.gelu(x, approximate=True)

def _silu(x):
    return jax.nn.silu(x)

def _sigmoid(x):
    return jax.nn.sigmoid(x)

def _layernorm(x, axis=-1, eps=1e-05):
    m = jnp.mean(x, axis=axis, keepdims=True)
    v = jnp.var(x, axis=axis, keepdims=True)
    return (x - m) / jnp.sqrt(v + eps)

def _scatter_add(tgt, idx, src, axis=0):
    return tgt.at[idx].add(src)

def _segment_sum(src, seg, n):
    return jax.ops.segment_sum(src, seg, n)
kernel_name = 'mk_macaron_d2_jaxref_r8_4deeea'

def setup_inputs(seed: int=0):
    np.random.seed(seed)
    _w = jnp.asarray

    def _L0_attn_setup():
        import jax, jax.numpy as jnp
        import numpy as np
        N_HEAD = 16
        ROPE_THETA = 10000.0

        def _rope(x):
            T, D = (x.shape[-2], x.shape[-1])
            inv_freq = 1.0 / ROPE_THETA ** (jnp.arange(0, D, 2, dtype=jnp.float32) / D)
            freqs = jnp.arange(T, dtype=jnp.float32)[:, None] * inv_freq[None, :]
            emb = jnp.repeat(freqs, 2, axis=-1)
            cos, sin = (jnp.cos(emb), jnp.sin(emb))
            xr = x.reshape(*x.shape[:-1], D // 2, 2)
            x1, x2 = (xr[..., 0], xr[..., 1])
            rot = jnp.stack((-x2, x1), axis=-1).reshape(x.shape)
            return x * cos + rot * sin
        key = jax.random.key(seed)
        k0, k1, k2 = jax.random.split(key, 3)
        B, T, C = (2, 256, 128)
        s = 0.02
        return {'x': jax.random.normal(k0, (B, T, C), jnp.float32), 'w_attn': jax.random.normal(k1, (C, 3 * C), jnp.float32) * s, 'b_attn': jnp.zeros((3 * C,), jnp.float32), 'w_proj': jax.random.normal(k2, (C, C), jnp.float32) * s, 'b_proj': jnp.zeros((C,), jnp.float32)}
    _L0_attn_in = _L0_attn_setup()

    def _L0_ffn_setup():
        import jax, jax.numpy as jnp
        import numpy as np
        DIM = 128
        HIDDEN = 512
        E = 8
        B, S = (2, 512)
        key = jax.random.key(seed)
        ks = jax.random.split(key, 8)
        sd = 1.0 / np.sqrt(DIM)
        sh = 1.0 / np.sqrt(HIDDEN)
        return {'x': jax.random.normal(ks[0], (B, S, DIM), dtype=jnp.float32), 'router_w': jax.random.uniform(ks[1], (DIM, E), jnp.float32, -sd, sd), 'router_b': jax.random.uniform(ks[2], (E,), jnp.float32, -sd, sd), 'w1': jax.random.uniform(ks[3], (E, DIM, 2 * HIDDEN), jnp.float32, -sd, sd), 'b1': jax.random.uniform(ks[4], (E, 2 * HIDDEN), jnp.float32, -sd, sd), 'w2': jax.random.uniform(ks[5], (E, HIDDEN, DIM), jnp.float32, -sh, sh), 'b2': jax.random.uniform(ks[6], (E, DIM), jnp.float32, -sh, sh)}
    _L0_ffn_in = _L0_ffn_setup()

    def _L1_attn_setup():
        import jax, jax.numpy as jnp
        import numpy as np
        B, T, C, H = (2, 256, 128, 16)
        DH = C // H
        EPS = 1e-05

        def _rotary(t_len, d_head):
            inv_freq = 1.0 / 10000.0 ** (jnp.arange(0, d_head, 2, dtype=jnp.float32) / d_head)
            t = jnp.arange(t_len, dtype=jnp.float32)
            freqs = t[:, None] * inv_freq[None, :]
            emb = jnp.concatenate([freqs, freqs], axis=-1)
            return (jnp.cos(emb), jnp.sin(emb))

        def _apply_rope(x, cos, sin):
            d = x.shape[-1]
            x1, x2 = (x[..., :d // 2], x[..., d // 2:])
            x_rot = jnp.concatenate([-x2, x1], axis=-1)
            return x * cos + x_rot * sin

        def _decay_mask(t_len, n_head):
            gammas = 1.0 - 2.0 ** (-5.0 - jnp.arange(n_head, dtype=jnp.float32))
            n = jnp.arange(t_len)[:, None]
            m = jnp.arange(t_len)[None, :]
            dist = n - m
            decay = gammas[:, None, None] ** jnp.maximum(dist, 0).astype(jnp.float32)
            return jnp.where(dist[None] >= 0, decay, 0.0)
        key = jax.random.key(seed)
        ks = jax.random.split(key, 7)
        s = 1.0 / np.sqrt(C)
        return {'x': jax.random.normal(ks[0], (B, T, C), dtype=jnp.float32), 'Wq': jax.random.normal(ks[1], (C, C), dtype=jnp.float32) * s, 'Wk': jax.random.normal(ks[2], (C, C), dtype=jnp.float32) * s, 'Wv': jax.random.normal(ks[3], (C, C), dtype=jnp.float32) * s, 'Wo': jax.random.normal(ks[4], (C, C), dtype=jnp.float32) * s, 'gn_weight': jnp.ones((C,), dtype=jnp.float32), 'gn_bias': jnp.zeros((C,), dtype=jnp.float32)}
    _L1_attn_in = _L1_attn_setup()

    def _L1_ffn_setup():
        import jax, jax.numpy as jnp
        import numpy as np
        DIM = 128
        DEPTH = 2
        HEADS = 8
        DIM_HEAD = 64
        WINDOW = 64
        INNER = HEADS * DIM_HEAD
        HID = int(DIM * 4 * 2 / 3)
        B, N = (2, 1024)
        QK_SCALE = 8.0

        def shift_token(t):
            t1, t2 = jnp.split(t, 2, axis=-1)
            t2 = jnp.pad(t2, ((0, 0), (1, 0), (0, 0)))[:, :-1]
            return jnp.concatenate([t1, t2], axis=-1)

        def l2norm(t):
            return t / jnp.clip(jnp.linalg.norm(t, axis=-1, keepdims=True), 1e-12)

        def rotate_half(x):
            x1, x2 = jnp.split(x, 2, axis=-1)
            return jnp.concatenate([-x2, x1], axis=-1)

        def rotary_xpos(q, k):
            n = q.shape[-2]
            half_idx = jnp.arange(0, DIM_HEAD, 2, dtype=jnp.float32)
            inv_freq = 1.0 / 10000.0 ** (half_idx / DIM_HEAD)
            t = jnp.arange(n, dtype=jnp.float32)
            freqs = t[:, None] * inv_freq[None, :]
            freqs = jnp.concatenate([freqs, freqs], axis=-1)
            base = (half_idx + 0.4 * DIM_HEAD) / (1.4 * DIM_HEAD)
            power = (t - n // 2) / float(WINDOW // 2)
            scale = base[None, :] ** power[:, None]
            scale = jnp.concatenate([scale, scale], axis=-1)
            cos, sin = (jnp.cos(freqs), jnp.sin(freqs))
            q = q * cos * scale + rotate_half(q) * sin * scale
            k = k * cos / scale + rotate_half(k) * sin / scale
            return (q, k)

        def local_attention(q, k, v):
            b, h, n, d = q.shape
            w = n // WINDOW
            bq = q.reshape(b, h, w, WINDOW, d) * QK_SCALE
            bk = k.reshape(b, h, w, WINDOW, d)
            bv = v.reshape(b, h, w, WINDOW, d)

            def look_around(t):
                p = jnp.pad(t, ((0, 0), (0, 0), (1, 0), (0, 0), (0, 0)))
                return jnp.concatenate([p[:, :, :w], p[:, :, 1:]], axis=3)
            bk, bv = (look_around(bk), look_around(bv))
            bt = jnp.arange(n).reshape(w, WINDOW)
            btp = jnp.pad(bt, ((1, 0), (0, 0)), constant_values=-1)
            btk = jnp.concatenate([btp[:w], btp[1:]], axis=1)
            sim = jnp.einsum('bhwid,bhwjd->bhwij', bq, bk)
            i = bt[:, :, None]
            j = btk[:, None, :]
            mask = (i < j) | (i > j + WINDOW) | (j == -1)
            sim = jnp.where(mask, -jnp.finfo(sim.dtype).max, sim)
            attn = jax.nn.softmax(sim, axis=-1)
            out = jnp.einsum('bhwij,bhwjd->bhwid', attn, bv)
            return out.reshape(b, h, n, d)

        def _layer(x, wqkv, qs, ksc, wo, lg, lb, w1, b1, w2, b2):
            b, n, _ = x.shape
            h = shift_token(x)
            qkv = h @ wqkv
            q, k, v = jnp.split(qkv, 3, axis=-1)
            to_heads = lambda t: t.reshape(b, n, HEADS, DIM_HEAD).transpose(0, 2, 1, 3)
            q, k, v = (to_heads(q), to_heads(k), to_heads(v))
            q = l2norm(q) * qs
            k = l2norm(k) * ksc
            q, k = rotary_xpos(q, k)
            o = local_attention(q, k, v)
            o = o.transpose(0, 2, 1, 3).reshape(b, n, INNER)
            x = x + o @ wo
            h = shift_token(x)
            mu = h.mean(-1, keepdims=True)
            var = h.var(-1, keepdims=True)
            h = (h - mu) / jnp.sqrt(var + 1e-05) * lg + lb
            h = h @ w1 + b1
            a, g = jnp.split(h, 2, axis=-1)
            h = a * jax.nn.gelu(g, approximate=False)
            x = x + h @ w2 + b2
            return x
        key = jax.random.key(seed)
        ks = jax.random.split(key, 6)
        return {'x': jax.random.normal(ks[0], (B, N, DIM), jnp.float32), 'wqkv': jax.random.normal(ks[1], (DEPTH, DIM, 3 * INNER), jnp.float32) * 0.02, 'q_scale': jnp.ones((DEPTH, DIM_HEAD), jnp.float32), 'k_scale': jnp.ones((DEPTH, DIM_HEAD), jnp.float32), 'wo': jax.random.normal(ks[2], (DEPTH, INNER, DIM), jnp.float32) * 0.02, 'ln_g': jnp.ones((DEPTH, DIM), jnp.float32), 'ln_b': jnp.zeros((DEPTH, DIM), jnp.float32), 'w1': jax.random.normal(ks[3], (DEPTH, DIM, 2 * HID), jnp.float32) * 0.02, 'b1': jnp.zeros((DEPTH, 2 * HID), jnp.float32), 'w2': jax.random.normal(ks[4], (DEPTH, HID, DIM), jnp.float32) * 0.02, 'b2': jnp.zeros((DEPTH, DIM), jnp.float32)}
    _L1_ffn_in = _L1_ffn_setup()
    _d = {'L0_attn_x': _L0_attn_in['x'], 'L0_attn_w_attn': _L0_attn_in['w_attn'], 'L0_attn_b_attn': _L0_attn_in['b_attn'], 'L0_attn_w_proj': _L0_attn_in['w_proj'], 'L0_attn_b_proj': _L0_attn_in['b_proj'], 'L0_ffn_router_w': _L0_ffn_in['router_w'], 'L0_ffn_router_b': _L0_ffn_in['router_b'], 'L0_ffn_w1': _L0_ffn_in['w1'], 'L0_ffn_b1': _L0_ffn_in['b1'], 'L0_ffn_w2': _L0_ffn_in['w2'], 'L0_ffn_b2': _L0_ffn_in['b2'], 'L1_attn_Wq': _L1_attn_in['Wq'], 'L1_attn_Wk': _L1_attn_in['Wk'], 'L1_attn_Wv': _L1_attn_in['Wv'], 'L1_attn_Wo': _L1_attn_in['Wo'], 'L1_attn_gn_weight': _L1_attn_in['gn_weight'], 'L1_attn_gn_bias': _L1_attn_in['gn_bias'], 'L1_ffn_wqkv': _L1_ffn_in['wqkv'], 'L1_ffn_q_scale': _L1_ffn_in['q_scale'], 'L1_ffn_k_scale': _L1_ffn_in['k_scale'], 'L1_ffn_wo': _L1_ffn_in['wo'], 'L1_ffn_ln_g': _L1_ffn_in['ln_g'], 'L1_ffn_ln_b': _L1_ffn_in['ln_b'], 'L1_ffn_w1': _L1_ffn_in['w1'], 'L1_ffn_b1': _L1_ffn_in['b1'], 'L1_ffn_w2': _L1_ffn_in['w2'], 'L1_ffn_b2': _L1_ffn_in['b2']}
    _x0 = _d['L0_attn_x']
    _d['L0_attn_x'] = jax.random.normal(jax.random.fold_in(jax.random.key(seed), 1), (16, 256, 128), dtype=_x0.dtype)
    del _x0
    return _d

def reference(L0_attn_x, L0_attn_w_attn, L0_attn_b_attn, L0_attn_w_proj, L0_attn_b_proj, L0_ffn_router_w, L0_ffn_router_b, L0_ffn_w1, L0_ffn_b1, L0_ffn_w2, L0_ffn_b2, L1_attn_Wq, L1_attn_Wk, L1_attn_Wv, L1_attn_Wo, L1_attn_gn_weight, L1_attn_gn_bias, L1_ffn_wqkv, L1_ffn_q_scale, L1_ffn_k_scale, L1_ffn_wo, L1_ffn_ln_g, L1_ffn_ln_b, L1_ffn_w1, L1_ffn_b1, L1_ffn_w2, L1_ffn_b2):

    def _L0_attn_ref(x, w_attn, b_attn, w_proj, b_proj):
        import jax, jax.numpy as jnp
        import numpy as np
        N_HEAD = 16
        ROPE_THETA = 10000.0

        def _rope(x):
            T, D = (x.shape[-2], x.shape[-1])
            inv_freq = 1.0 / ROPE_THETA ** (jnp.arange(0, D, 2, dtype=jnp.float32) / D)
            freqs = jnp.arange(T, dtype=jnp.float32)[:, None] * inv_freq[None, :]
            emb = jnp.repeat(freqs, 2, axis=-1)
            cos, sin = (jnp.cos(emb), jnp.sin(emb))
            xr = x.reshape(*x.shape[:-1], D // 2, 2)
            x1, x2 = (xr[..., 0], xr[..., 1])
            rot = jnp.stack((-x2, x1), axis=-1).reshape(x.shape)
            return x * cos + rot * sin
        B, T, C = x.shape
        H = N_HEAD
        D = C // H
        qkv = x @ w_attn + b_attn
        q, k, v = jnp.split(qkv, 3, axis=-1)

        def heads(t):
            return t.reshape(B, T, H, D).transpose(0, 2, 1, 3)
        q, k, v = (heads(q), heads(k), heads(v))
        q = _rope(q)
        k = _rope(k)
        att = jnp.einsum('bhqd,bhkd->bhqk', q, k) * (1.0 / np.sqrt(D))
        causal = jnp.tril(jnp.ones((T, T), dtype=bool))
        att = jnp.where(causal, att, -jnp.inf)
        att = jax.nn.softmax(att, axis=-1)
        y = jnp.einsum('bhqk,bhkd->bhqd', att, v)
        y = y.transpose(0, 2, 1, 3).reshape(B, T, C)
        return y @ w_proj + b_proj

    def _L0_ffn_ref(x, router_w, router_b, w1, b1, w2, b2):
        import jax, jax.numpy as jnp
        import numpy as np
        DIM = 128
        HIDDEN = 512
        E = 8
        B, S = (2, 512)
        logits = jnp.einsum('bsd,de->bse', x, router_w) + router_b
        probs = jax.nn.softmax(logits, axis=-1)
        top1 = jnp.argmax(probs, axis=-1)
        out = jnp.zeros_like(x)
        for i in range(E):
            h = jnp.einsum('bsd,df->bsf', x, w1[i]) + b1[i]
            a, g = jnp.split(h, 2, axis=-1)
            y = jnp.einsum('bsh,hd->bsd', a * jax.nn.sigmoid(g), w2[i]) + b2[i]
            out = out + jnp.where((top1 == i)[..., None], y, 0.0)
        return out

    def _L1_attn_ref(x, Wq, Wk, Wv, Wo, gn_weight, gn_bias):
        import jax, jax.numpy as jnp
        import numpy as np
        B, T, C, H = (2, 256, 128, 16)
        DH = C // H
        EPS = 1e-05

        def _rotary(t_len, d_head):
            inv_freq = 1.0 / 10000.0 ** (jnp.arange(0, d_head, 2, dtype=jnp.float32) / d_head)
            t = jnp.arange(t_len, dtype=jnp.float32)
            freqs = t[:, None] * inv_freq[None, :]
            emb = jnp.concatenate([freqs, freqs], axis=-1)
            return (jnp.cos(emb), jnp.sin(emb))

        def _apply_rope(x, cos, sin):
            d = x.shape[-1]
            x1, x2 = (x[..., :d // 2], x[..., d // 2:])
            x_rot = jnp.concatenate([-x2, x1], axis=-1)
            return x * cos + x_rot * sin

        def _decay_mask(t_len, n_head):
            gammas = 1.0 - 2.0 ** (-5.0 - jnp.arange(n_head, dtype=jnp.float32))
            n = jnp.arange(t_len)[:, None]
            m = jnp.arange(t_len)[None, :]
            dist = n - m
            decay = gammas[:, None, None] ** jnp.maximum(dist, 0).astype(jnp.float32)
            return jnp.where(dist[None] >= 0, decay, 0.0)
        b, t, c = x.shape

        def proj(W):
            return jnp.einsum('btc,oc->bto', x, W).reshape(b, t, H, DH).transpose(0, 2, 1, 3)
        q, k, v = (proj(Wq), proj(Wk), proj(Wv))
        cos, sin = _rotary(t, DH)
        q = _apply_rope(q, cos, sin)
        k = _apply_rope(k, cos, sin)
        decay = _decay_mask(t, H)
        qk = jnp.einsum('bhtd,bhsd->bhts', q, k) * (1.0 / np.sqrt(DH))
        qk = qk * decay[None]
        out = jnp.einsum('bhts,bhsd->bhtd', qk, v)
        out = out.transpose(0, 2, 1, 3)
        mu = jnp.mean(out, axis=-1, keepdims=True)
        var = jnp.mean((out - mu) ** 2, axis=-1, keepdims=True)
        out = (out - mu) * jax.lax.rsqrt(var + EPS)
        out = out * gn_weight.reshape(H, DH) + gn_bias.reshape(H, DH)
        out = out.reshape(b, t, c)
        return jnp.einsum('btc,oc->bto', out, Wo)

    def _L1_ffn_ref(x, wqkv, q_scale, k_scale, wo, ln_g, ln_b, w1, b1, w2, b2):
        import jax, jax.numpy as jnp
        import numpy as np
        DIM = 128
        DEPTH = 2
        HEADS = 8
        DIM_HEAD = 64
        WINDOW = 64
        INNER = HEADS * DIM_HEAD
        HID = int(DIM * 4 * 2 / 3)
        B, N = (2, 1024)
        QK_SCALE = 8.0

        def shift_token(t):
            t1, t2 = jnp.split(t, 2, axis=-1)
            t2 = jnp.pad(t2, ((0, 0), (1, 0), (0, 0)))[:, :-1]
            return jnp.concatenate([t1, t2], axis=-1)

        def l2norm(t):
            return t / jnp.clip(jnp.linalg.norm(t, axis=-1, keepdims=True), 1e-12)

        def rotate_half(x):
            x1, x2 = jnp.split(x, 2, axis=-1)
            return jnp.concatenate([-x2, x1], axis=-1)

        def rotary_xpos(q, k):
            n = q.shape[-2]
            half_idx = jnp.arange(0, DIM_HEAD, 2, dtype=jnp.float32)
            inv_freq = 1.0 / 10000.0 ** (half_idx / DIM_HEAD)
            t = jnp.arange(n, dtype=jnp.float32)
            freqs = t[:, None] * inv_freq[None, :]
            freqs = jnp.concatenate([freqs, freqs], axis=-1)
            base = (half_idx + 0.4 * DIM_HEAD) / (1.4 * DIM_HEAD)
            power = (t - n // 2) / float(WINDOW // 2)
            scale = base[None, :] ** power[:, None]
            scale = jnp.concatenate([scale, scale], axis=-1)
            cos, sin = (jnp.cos(freqs), jnp.sin(freqs))
            q = q * cos * scale + rotate_half(q) * sin * scale
            k = k * cos / scale + rotate_half(k) * sin / scale
            return (q, k)

        def local_attention(q, k, v):
            b, h, n, d = q.shape
            w = n // WINDOW
            bq = q.reshape(b, h, w, WINDOW, d) * QK_SCALE
            bk = k.reshape(b, h, w, WINDOW, d)
            bv = v.reshape(b, h, w, WINDOW, d)

            def look_around(t):
                p = jnp.pad(t, ((0, 0), (0, 0), (1, 0), (0, 0), (0, 0)))
                return jnp.concatenate([p[:, :, :w], p[:, :, 1:]], axis=3)
            bk, bv = (look_around(bk), look_around(bv))
            bt = jnp.arange(n).reshape(w, WINDOW)
            btp = jnp.pad(bt, ((1, 0), (0, 0)), constant_values=-1)
            btk = jnp.concatenate([btp[:w], btp[1:]], axis=1)
            sim = jnp.einsum('bhwid,bhwjd->bhwij', bq, bk)
            i = bt[:, :, None]
            j = btk[:, None, :]
            mask = (i < j) | (i > j + WINDOW) | (j == -1)
            sim = jnp.where(mask, -jnp.finfo(sim.dtype).max, sim)
            attn = jax.nn.softmax(sim, axis=-1)
            out = jnp.einsum('bhwij,bhwjd->bhwid', attn, bv)
            return out.reshape(b, h, n, d)

        def _layer(x, wqkv, qs, ksc, wo, lg, lb, w1, b1, w2, b2):
            b, n, _ = x.shape
            h = shift_token(x)
            qkv = h @ wqkv
            q, k, v = jnp.split(qkv, 3, axis=-1)
            to_heads = lambda t: t.reshape(b, n, HEADS, DIM_HEAD).transpose(0, 2, 1, 3)
            q, k, v = (to_heads(q), to_heads(k), to_heads(v))
            q = l2norm(q) * qs
            k = l2norm(k) * ksc
            q, k = rotary_xpos(q, k)
            o = local_attention(q, k, v)
            o = o.transpose(0, 2, 1, 3).reshape(b, n, INNER)
            x = x + o @ wo
            h = shift_token(x)
            mu = h.mean(-1, keepdims=True)
            var = h.var(-1, keepdims=True)
            h = (h - mu) / jnp.sqrt(var + 1e-05) * lg + lb
            h = h @ w1 + b1
            a, g = jnp.split(h, 2, axis=-1)
            h = a * jax.nn.gelu(g, approximate=False)
            x = x + h @ w2 + b2
            return x
        for l in range(DEPTH):
            x = _layer(x, wqkv[l], q_scale[l], k_scale[l], wo[l], ln_g[l], ln_b[l], w1[l], b1[l], w2[l], b2[l])
        return x
    x = L0_attn_x
    x = x + 0.5 * _L0_ffn_ref(_layernorm(x, axis=-1), L0_ffn_router_w, L0_ffn_router_b, L0_ffn_w1, L0_ffn_b1, L0_ffn_w2, L0_ffn_b2)
    x = x + _L0_attn_ref(_layernorm(x, axis=-1), L0_attn_w_attn, L0_attn_b_attn, L0_attn_w_proj, L0_attn_b_proj)
    x = x + 0.5 * _L0_ffn_ref(_layernorm(x, axis=-1), L0_ffn_router_w, L0_ffn_router_b, L0_ffn_w1, L0_ffn_b1, L0_ffn_w2, L0_ffn_b2)
    x = x + 0.5 * _L1_ffn_ref(_layernorm(x, axis=-1), L1_ffn_wqkv, L1_ffn_q_scale, L1_ffn_k_scale, L1_ffn_wo, L1_ffn_ln_g, L1_ffn_ln_b, L1_ffn_w1, L1_ffn_b1, L1_ffn_w2, L1_ffn_b2)
    x = x + _L1_attn_ref(_layernorm(x, axis=-1), L1_attn_Wq, L1_attn_Wk, L1_attn_Wv, L1_attn_Wo, L1_attn_gn_weight, L1_attn_gn_bias)
    x = x + 0.5 * _L1_ffn_ref(_layernorm(x, axis=-1), L1_ffn_wqkv, L1_ffn_q_scale, L1_ffn_k_scale, L1_ffn_wo, L1_ffn_ln_g, L1_ffn_ln_b, L1_ffn_w1, L1_ffn_b1, L1_ffn_w2, L1_ffn_b2)
    return x

_drawn_inputs = setup_inputs


def setup_inputs(seed=0):
    import zlib

    import numpy as np

    out = dict(_drawn_inputs(seed))
    spreads = {'L0_attn_b_attn': (0.0, 0.1),
     'L0_attn_b_proj': (0.0, 0.1),
     'L1_attn_gn_weight': (1.0, 0.2),
     'L1_attn_gn_bias': (0.0, 0.411),
     'L1_ffn_q_scale': (1.0, 0.6),
     'L1_ffn_k_scale': (1.0, 0.6),
     'L1_ffn_ln_g': (1.0, 0.6),
     'L1_ffn_ln_b': (0.0, 0.8),
     'L1_ffn_b1': (0.0, 0.8),
     'L1_ffn_b2': (0.0, 0.299)}
    factors = {'L1_ffn_w1': 5.507, 'L1_ffn_w2': 5.648, 'L0_attn_w_attn': 3.655}
    for name, (base, spread) in spreads.items():
        noise = np.random.default_rng([zlib.crc32(name.encode()), seed]).standard_normal(out[name].shape)
        drawn = base * np.exp(spread * noise) if base else spread * noise
        out[name] = jnp.asarray(drawn.astype(out[name].dtype))
    for name, factor in factors.items():
        out[name] = (out[name] * factor).astype(out[name].dtype)
    return out
```

```python
import numpy as np
from contextlib import ExitStack

import concourse.bass as bass
from concourse import mybir

F32 = mybir.dt.float32
BF16 = mybir.dt.bfloat16
ACT = mybir.ActivationFunctionType
ALU = mybir.AluOpType
AX = mybir.AxisListType

P = 128
B, T = 16, 256
N = B * T
MASKED = -1e30

LH, LD, WIN = 8, 64, 64
CH = LH // 2
BAND = 320
EPS = 1e-5
LN_EXP = "natural_log_exp_and_others"
HID = int(P * 4 * 2 / 3)
HCH = [(0, 128), (128, 128), (256, HID - 256)]


class Shared:

    def __init__(self):
        self.n = 0


def ds(start, size):
    return bass.ds(start, size)


def rounds(eng, first, count, tail, body):
    for i in range(first):
        body(i)
    with eng.Fori(first, count) as i:
        body(i)
    for i in range(count, count + tail):
        body(i)


def clear(nc, sems):
    with nc.Block() as block:
        @block.sync
        def _(sp):
            for x in sems:
                sp.sem_clear(x)


def runs(u, total):
    return not isinstance(u, int) or 0 <= u < total


def at_least(u, n):
    return not isinstance(u, int) or u >= n


def local_attention(nc, g, layer):
    U = B * CH
    wq, wo, tab = g.l1_wqkv[layer], g.l1_wo[layer], g.l1_tab[layer]
    qk_ps, rot_ps, v_ps, m1, m2, ol = g.bank[0], g.bank[1], g.bank[2], (g.bank[3], g.bank[4]), (g.bank[5], g.bank[6]), g.bank[7]
    with ExitStack() as ctx:
        def sb(name, shape, dt=F32):
            return ctx.enter_context(nc.sbuf_tensor(f"la{g.n}_{name}", shape, dt))

        sems = []

        def sem(name):
            sems.append(ctx.enter_context(nc.semaphore(f"la_{name}")))
            return sems[-1]
        g.n += 1
        hT = sb("hT", [P, 2, T])
        sq = sb("sq", [P, 2 * T])
        t1 = sb("t1", [P, 2 * T])
        t2 = sb("t2", [P, 2 * T])
        t3 = sb("t3", [P, 2 * T])
        lnn = sb("lnn", [P, 2 * T])
        rn = sb("rn", [P, 2 * T])
        qk = sb("qk", [P, CH, 2 * T])
        v = sb("v", [P, CH, 2, P])
        mx = sb("mx", [P, 2, 2])
        mp = sb("mp", [P, 2, 2, 2], BF16)
        mrow = sb("mrow", [4, T], BF16)
        pr = sb("pr", [P, 2, BAND])
        rl = sb("rl", [P, T])
        oT = sb("oT", [P, CH, T])
        h_ready, proj_ready, sq_ready, v_ready = sem("h_ready"), sem("proj_ready"), sem("sq_ready"), sem("v_ready")
        turned, summed, ss_ready, ln_ready, rn_ready = sem("turned"), sem("summed"), sem("ss_ready"), sem("ln_ready"), sem("rn_ready")
        qk_ready, s1_ready, mx_done, hi_done, mx_ready = sem("qk_ready"), sem("s1_ready"), sem("mx_done"), sem("hi_done"), sem("mx_ready")
        mT_ready, mrow_ready, s2_ready, p_ready = sem("mT_ready"), sem("mrow_ready"), sem("s2_ready"), sem("p_ready")
        ol_ready, rl_done, o_ready, zo_ready, z_ready = sem("ol_ready"), sem("rl_done"), sem("o_ready"), sem("zo_ready"), sem("z_ready")
        h_zero, h_low = sem("h_zero"), sem("h_low")
        ctx.callback(clear, nc, sems)
        block = ctx.enter_context(nc.Block())
        mm = nc.tensor.matmul

        @block.tensor
        def _(pe):
            def body(i):
                for j in range(CH):
                    s = CH * i + j
                    even = None
                    u = s - 3
                    if runs(u, U):
                        pe.wait_ge(mx_ready, u + 1)
                        if at_least(u, 1):
                            pe.wait_ge(p_ready, u)
                        mT = m2[0][0:4, 0:P].bitcast(BF16)
                        for t in range(2):
                            ins = nc.tensor.transpose(mT[:, t * P:(t + 1) * P], mp[:, t, :, :].rearrange("p a h -> p (a h)"), g.ident[:, :])
                        ins.then_inc(mT_ready, 1)
                    u = s - 4
                    if runs(u, U):
                        c = (j - 4) % CH
                        pe.wait_ge(p_ready, u + 1)
                        pe.wait_ge(v_ready, u + 1)
                        if at_least(u, 1):
                            pe.wait_ge(o_ready, u)
                        for part in range(2):
                            for kt, (q0, col, n) in enumerate(((0, 0, 192), (128, 192, 128))):
                                for h in range(2):
                                    w = v[:, c, kt, h * LD:(h + 1) * LD] if part == 0 else g.ones[:, 0:LD]
                                    ins = mm(ol[h * LD:(h + 1) * LD, part * T + q0:part * T + q0 + n], w, pr[:, h, col:col + n],
                                             start=(part == 0 and kt == 0), stop=(kt == 1), skip_group_check=True)
                        ins.then_inc(ol_ready, 1)
                    u = s - 2
                    if runs(u, U):
                        c = (j - 2) % CH
                        pe.wait_ge(qk_ready, u + 1)
                        if at_least(u, 1):
                            pe.wait_ge(mx_done, u)
                        for h in range(2):
                            r = slice(h * LD, (h + 1) * LD)
                            mm(m1[h][:, 0:BAND], g.ident[:, :], g.band_q[:, :], start=True, stop=False, skip_group_check=True)
                            mm(m1[h][:, 0:128], qk[r, c, 0:128], qk[r, c, T:T + 128], start=False, stop=False, skip_group_check=True)
                            ins = mm(m1[h][:, 128:BAND], qk[r, c, 128:256], qk[r, c, T + 64:T + 256], start=False, stop=True, skip_group_check=True)
                        ins.then_inc(s1_ready, 1)
                    u = s - 1
                    if runs(u, U):
                        pe.wait_ge(sq_ready, u + 1)
                        pe.wait_ge(turned, u + 1)
                        mm(qk_ps[:, :], g.head64[:, :], sq[:, :], start=True, stop=True).then_inc(ss_ready, 1)
                    u = s - 3
                    if runs(u, U):
                        c = (j - 3) % CH
                        pe.wait_ge(mrow_ready, u + 1)
                        for h in range(2):
                            r = slice(h * LD, (h + 1) * LD)
                            mm(m2[h][:, 0:BAND], g.ident[:, :], g.band_k[:, :], start=True, stop=False, skip_group_check=True)
                            mm(m2[h][:, 0:192], g.pick2[:, h, :], mrow[:, 0:192], start=False, stop=False, skip_group_check=True)
                            mm(m2[h][:, 192:BAND], g.pick2[:, h, :], mrow[:, 128:256], start=False, stop=False, skip_group_check=True)
                            mm(m2[h][:, 0:192], qk[r, c, T:T + 128], qk[r, c, 0:192], start=False, stop=False, skip_group_check=True)
                            ins = mm(m2[h][:, 192:BAND], qk[r, c, T + 128:T + 256], qk[r, c, 128:256], start=False, stop=True, skip_group_check=True)
                        ins.then_inc(s2_ready, 1)
                    if j == CH - 1 and runs(i - 1, B):
                        pe.wait_ge(o_ready, CH * i)
                        pe.wait_ge(turned, CH * i + j if not isinstance(i, int) else min(CH * i + j, U))
                        for c in range(CH):
                            ins = mm(rot_ps[:, 0:T], wo[:, c, :], oT[:, c, :], start=(c == 0), stop=(c == CH - 1))
                        ins.then_inc(zo_ready, 1)
                    if runs(s, U):
                        pe.wait_ge(h_ready, i + 1)
                        if at_least(s, 1):
                            pe.wait_ge(ln_ready, s)
                            pe.wait_ge(v_ready, s)
                            pe.wait_ge(turned, s)
                        hb = hbuf(i)
                        for k in range(2):
                            mm(qk_ps[:, k * T:(k + 1) * T], wq[:, k, j, :], hT[:, 0, :], start=(k == 0), stop=(k == 1), skip_group_check=True)
                        for t in range(2):
                            mm(v_ps[:, t * P:(t + 1) * P], hT[:, 0, t * P:(t + 1) * P], wq[:, 2, j, :], start=(t == 0), stop=(t == 1), skip_group_check=True)
                        if j == CH - 1 and runs(i - 1, B):
                            pe.wait_ge(z_ready, i)
                        for k in range(2):
                            ins = mm(rot_ps[:, k * T:(k + 1) * T], wq[:, 3 + k, j, :], hT[:, 0, :], start=(k == 0), stop=(k == 1), skip_group_check=True)
                        ins.then_inc(proj_ready, 1)

            def hbuf(i):
                return 0
            rounds(pe, 2, B, 1, body)

        @block.gpsimd
        def _(pool):
            pool.memset(hT[64:P, 0, 0:1], 0.0).then_inc(h_zero, 1)

            def body(i):
                for j in range(CH):
                    s = CH * i + j
                    u = s - 1
                    if runs(u, U):
                        pool.wait_ge(turned, u + 1)
                        if at_least(u, 1):
                            pool.wait_ge(qk_ready, u)
                        pool.tensor_tensor(t3[:, :], t1[:, :], t2[:, :], ALU.add).then_inc(summed, 1)
                    if j == 0 and runs(i, B):
                        if at_least(i, 1):
                            pool.wait_ge(proj_ready, CH * i)
                        z = g.z[:, ds(i * T, T)] if not isinstance(i, int) else g.z[:, i * T:(i + 1) * T]
                        if at_least(i, 1):
                            pool.wait_ge(summed, CH * i)
                        pool.tensor_copy(hT[0:64, 0, :], z[0:64, :]).then_inc(h_low, 1)
                        pool.wait_ge(h_low, i + 1)
                        pool.tensor_copy(hT[64:P, 0, 1:T], z[64:P, 0:T - 1]).then_inc(h_ready, 1)
                        pool.wait_ge(h_ready, i + 1)
            pool.wait_ge(h_zero, 1)
            rounds(pool, 2, B, 1, body)

        @block.scalar
        def _(act):
            act.preload_act_table_set(LN_EXP)

            def body(i):
                for j in range(CH):
                    s = CH * i + j
                    u = s - 1
                    if runs(u, U):
                        c = (j - 1) % CH
                        act.wait_ge(proj_ready, u + 1)
                        act.activation(sq[:, :], qk_ps[:, :], ACT.Square).then_inc(sq_ready, 1)
                        if at_least(u, 4):
                            act.wait_ge(ol_ready, u - 3)
                        act.activation(v[:, c, :, :].rearrange("p a b -> p (a b)"), v_ps[:, 0:T], ACT.Copy).then_inc(v_ready, 1)
                    u = s - 3
                    if runs(u, U):
                        act.wait_ge(mT_ready, u + 1)
                        if at_least(u, 1):
                            act.wait_ge(s2_ready, u)
                        act.activation(mrow[:, :], m2[0][0:4, 0:P].bitcast(BF16), ACT.Copy).then_inc(mrow_ready, 1)
                    u = s - 1
                    if runs(u, U):
                        act.wait_ge(ss_ready, u + 1)
                        act.activation(lnn[:, :], qk_ps[:, :], ACT.Ln, scale=float(2 ** 20), bias=g.tiny[:, 0:1]).then_inc(ln_ready, 1)
                        act.wait_ge(ln_ready, u + 1)
                        if at_least(u, 1):
                            act.wait_ge(qk_ready, u)
                        act.activation(rn[:, :], lnn[:, :], ACT.Exp, scale=-0.5, bias=g.tiny[:, 1:2]).then_inc(rn_ready, 1)
                    u = s - 3
                    if runs(u, U):
                        act.wait_ge(s2_ready, u + 1)
                        if at_least(u, 1):
                            act.wait_ge(ol_ready, u)
                        act.activation(pr[:, :, :], g.bank_pair5[:, :, 0:BAND], ACT.Exp).then_inc(p_ready, 1)
            rounds(act, 2, B, 1, body)

        @block.vector
        def _(dve):
            def body(i):
                for j in range(CH):
                    s = CH * i + j
                    u = s - 1
                    if runs(u, U):
                        dve.wait_ge(proj_ready, u + 1)
                        if at_least(u, 1):
                            dve.wait_ge(summed, u)
                        dve.tensor_tensor(t2[:, :], rot_ps[:, :], tab[:, 1, :], ALU.mult)
                        dve.wait_ge(sq_ready, u + 1)
                        dve.tensor_tensor(t1[:, :], qk_ps[:, :], tab[:, 0, :], ALU.mult).then_inc(turned, 1)
                    u = s - 4
                    if runs(u, U):
                        c = (j - 4) % CH
                        dve.wait_ge(ol_ready, u + 1)
                        dve.reciprocal(rl[:, :], ol[:, T:2 * T]).then_inc(rl_done, 1)
                        dve.wait_ge(rl_done, u + 1)
                        if c == 0 and at_least(u, 4):
                            dve.wait_ge(zo_ready, i - 1)
                        dve.tensor_tensor(oT[:, c, :], ol[:, 0:T], rl[:, :], ALU.mult).then_inc(o_ready, 1)
                    u = s - 2
                    if runs(u, U):
                        dve.wait_ge(s1_ready, u + 1)
                        dve.reduce_max(mx[:, 0, :], g.bank_pair3[:, :, 0:128], AX.X)
                        dve.reduce_max(mx[:, 1, :], g.bank_pair3[:, :, 128:BAND], AX.X).then_inc(mx_done, 1)
                        dve.wait_ge(mx_done, u + 1)
                        if at_least(u, 1):
                            dve.wait_ge(mT_ready, u)
                        dve.tensor_scalar(mp[:, :, 0, :], mx[:, :, :], -1.0, None, ALU.mult).then_inc(hi_done, 1)
                        dve.wait_ge(hi_done, u + 1)
                        dve.scalar_tensor_tensor(mp[:, :, 1, :], mx[:, :, :], -1.0, mp[:, :, 0, :], ALU.mult, ALU.subtract).then_inc(mx_ready, 1)
                    u = s - 1
                    if runs(u, U):
                        c = (j - 1) % CH
                        dve.wait_ge(rn_ready, u + 1)
                        dve.wait_ge(summed, u + 1)
                        if at_least(u, 4):
                            dve.wait_ge(s2_ready, u - 3)
                        dve.scalar_tensor_tensor(qk[:, c, :], rn[:, :], 1e12, t3[:, :], ALU.min, ALU.mult).then_inc(qk_ready, 1)
                    if j == CH - 1 and runs(i - 1, B):
                        dve.wait_ge(zo_ready, i)
                        b = i - 1
                        z = g.z[:, ds(b * T, T)] if not isinstance(i, int) else g.z[:, b * T:(b + 1) * T]
                        dve.tensor_tensor(z, rot_ps[:, 0:T], z, ALU.add).then_inc(z_ready, 1)
            rounds(dve, 2, B, 1, body)


def constants():
    f = {}
    eye = np.eye(P, dtype=np.float32)
    f["center"] = eye - np.float32(1 / P)
    f["mean"] = np.full((P, P), 1 / P, np.float32)
    ch = np.arange(P)
    f["head64"] = (ch[:, None] // LD == ch[None] // LD).astype(np.float32)
    f["ones"] = np.ones((P, P), np.float32)
    f["tiny"] = np.tile(np.array([1e-18, 10 * np.log(2.0), EPS, 0], np.float32), (P, 1))
    pos = np.arange(T, dtype=np.float32)
    half = np.arange(0, LD, 2, dtype=np.float32)
    inv = (1.0 / np.float32(10000.0) ** (half / np.float32(LD))).astype(np.float32)
    ang = (pos[:, None] * inv[None]).astype(np.float32).astype(np.float64)
    base = ((half + 0.4 * LD) / (1.4 * LD)).astype(np.float64)
    power = (pos - T // 2) / float(WIN // 2)
    sc = base[None] ** power[:, None].astype(np.float64)
    dd = ch % LD
    e = dd % (LD // 2)
    sign = np.where(dd < LD // 2, -1.0, 1.0)[:, None]
    c, s, x = np.cos(ang)[:, e].T, np.sin(ang)[:, e].T * sign, sc[:, e].T
    f["l1_base"] = np.stack([np.concatenate([c * x * 8.0, c / x], 1), np.concatenate([s * x * 8.0, s / x], 1)], 1)
    d8 = ch % SD
    inv8 = (1.0 / np.float32(10000.0) ** (np.arange(0, SD, 2, dtype=np.float32) / np.float32(SD))).astype(np.float32)
    ang8 = (pos[:, None] * inv8[None]).astype(np.float32).astype(np.float64)
    c, s = np.cos(ang8)[:, d8 // 2].T, np.sin(ang8)[:, d8 // 2].T * np.where(d8 % 2 == 0, -1.0, 1.0)[:, None]
    r8 = SD ** -0.5
    f["l0_tab"] = np.stack([np.concatenate([c * r8, c], 1), np.concatenate([s * r8, s], 1)], 1)
    c, s = np.cos(ang8)[:, d8 % 4].T, np.sin(ang8)[:, d8 % 4].T * np.where(d8 < 4, -1.0, 1.0)[:, None]
    gam = 1.0 - 2.0 ** (-5.0 - (ch // SD)[:, None])
    up, down = gam ** pos[None].astype(np.float64) * r8, gam ** -pos[None].astype(np.float64)
    f["r1_tab"] = np.stack([np.concatenate([c * up, c * down], 1), np.concatenate([s * up, s * down], 1)], 1)
    f["head_j"] = (ch[:, None] % 32 // SD == np.arange(4)[None]).astype(np.float32)
    f["ones_j"] = np.broadcast_to(np.arange(32)[None, None] // SD == np.arange(4)[None, :, None], (P, 4, 32))
    f["head_center"] = eye - (ch[:, None] // SD == ch[None] // SD) / SD
    f["head_mean"] = (ch[:, None] // SD == ch[None] // SD) / SD
    f["before"] = (ch[:, None] < ch[None]).astype(np.float32)
    b = {}
    b["ident"] = eye
    f["ident32"] = eye
    seen = np.triu(np.ones((P, P)))
    full = np.ones((P, P))
    f["tri_01"] = np.tile(np.concatenate([seen, full, seen], 1), (1, 2))
    b["tri_k"] = (1 - np.concatenate([seen, full, seen], 1)) * MASKED
    b["tri_q"] = (1 - np.concatenate([seen.T, full, seen.T], 1)) * MASKED
    f["down8"] = np.tile(8.0 - np.arange(8), (P, 1))
    f["block_of"] = np.tile(np.arange(BLOCKS), (P, 1))
    b["band_q"] = np.zeros((P, BAND))
    b["band_k"] = np.zeros((P, BAND))
    for p in range(P):
        for n in range(BAND):
            d = p - n if n < 128 else (128 + p) - (64 + n - 128)
            b["band_q"][p, n] = 0 if 0 <= d <= WIN else MASKED
            d = n - p if n < 192 else (128 + n - 192) - (128 + p)
            b["band_k"][p, n] = 0 if 0 <= d <= WIN else MASKED
    pick = np.zeros((P, 2, P))
    for h in range(2):
        pick[h, h] = 1
        pick[2 + h, h] = 1
    b["pick2"] = pick
    f = {k: np.ascontiguousarray(v.reshape(P, -1), np.float32) for k, v in f.items()}
    b = {k: v.reshape(P, -1) for k, v in b.items()}
    return f, b


def layer_norm(nc, g, src, dst, center, mean, shift=False, gain=None, bias=None):
    W = 2 * T
    U = N // W
    with ExitStack() as ctx:
        g.n += 1

        def sb(name, shape, dt=F32):
            return ctx.enter_context(nc.sbuf_tensor(f"ln{g.n}_{name}", shape, dt))

        sems = []

        def sem(name):
            sems.append(ctx.enter_context(nc.semaphore(f"ln_{name}")))
            return sems[-1]
        hb = sb("hb", [P, 2, W])
        sq = sb("sq", [P, 2, W])
        lnv = sb("lnv", [P, W])
        rstd = sb("rstd", [P, 2, W])
        normed = sb("normed", [P, W])
        h_zero, h_low, h_ready, c_ready, sq_ready = sem("h_zero"), sem("h_low"), sem("h_ready"), sem("c_ready"), sem("sq_ready")
        var_ready, ln_ready, r_ready, normed_ready, done = sem("var_ready"), sem("ln_ready"), sem("r_ready"), sem("normed_ready"), sem("done")
        ctx.callback(clear, nc, sems)
        block = ctx.enter_context(nc.Block())
        cb, vb = (g.bank[0], g.bank[1]), (g.bank[2], g.bank[3])

        def part(x, s):
            return x[:, ds(s * W, W)] if not isinstance(s, int) else x[:, s * W:(s + 1) * W]

        @block.gpsimd
        def _(pool):
            def body(i):
                for j in range(2):
                    s = 2 * i + j
                    if shift and runs(s, U):
                        if at_least(s, 2):
                            pool.wait_ge(c_ready, s - 1)
                        z = part(src, s).rearrange("p (b t) -> p b t", b=2)
                        h = hb[:, j, :].rearrange("p (b t) -> p b t", b=2)
                        pool.tensor_copy(h[0:64], z[0:64]).then_inc(h_low, 1)
                        pool.wait_ge(h_low, s + 1)
                        pool.tensor_copy(h[64:P, :, 1:T], z[64:P, :, 0:T - 1]).then_inc(h_ready, 1)
                        pool.wait_ge(h_ready, s + 1)
            if shift:
                pool.memset(hb[64:P, :, :].rearrange("p j (b t) -> p (j b) t", b=2)[:, :, 0:1], 0.0).then_inc(h_zero, 1)
                pool.wait_ge(h_zero, 1)
                rounds(pool, 1, U // 2, 0, body)

        @block.tensor
        def _(pe):
            def body(i):
                for j in range(2):
                    s = 2 * i + j
                    if runs(s, U):
                        if shift:
                            pe.wait_ge(h_ready, s + 1)
                        if at_least(s, 2):
                            pe.wait_ge(normed_ready, s - 1)
                        nc.tensor.matmul(cb[j], center, hb[:, j, :] if shift else part(src, s), start=True, stop=True).then_inc(c_ready, 1)
                    u = s - 1
                    if runs(u, U):
                        pe.wait_ge(sq_ready, u + 1)
                        if at_least(u, 2):
                            pe.wait_ge(ln_ready, u - 1)
                        nc.tensor.matmul(vb[1 - j], mean, sq[:, 1 - j, :], start=True, stop=True).then_inc(var_ready, 1)
            rounds(pe, 2, U // 2, 1, body)

        @block.scalar
        def _(act):
            act.preload_act_table_set(LN_EXP)

            def body(i):
                for j in range(2):
                    s = 2 * i + j
                    if runs(s, U):
                        act.wait_ge(c_ready, s + 1)
                        if at_least(s, 2):
                            act.wait_ge(var_ready, s - 1)
                        act.activation(sq[:, j, :], cb[j], ACT.Square).then_inc(sq_ready, 1)
                    u = s - 1
                    if runs(u, U):
                        act.wait_ge(var_ready, u + 1)
                        if at_least(u, 1):
                            act.wait_ge(r_ready, u)
                        act.activation(lnv[:, :], vb[1 - j], ACT.Ln, bias=g.tiny[:, 2:3]).then_inc(ln_ready, 1)
                        act.wait_ge(ln_ready, u + 1)
                        if at_least(u, 2):
                            act.wait_ge(normed_ready, u - 1)
                        act.activation(rstd[:, 1 - j, :], lnv[:, :], ACT.Exp, scale=-0.5).then_inc(r_ready, 1)
            rounds(act, 2, U // 2, 1, body)

        @block.vector
        def _(dve):
            def body(i):
                for j in range(2):
                    u = 2 * i + j - 1
                    if runs(u, U):
                        dve.wait_ge(r_ready, u + 1)
                        out = part(dst, u) if gain is None else normed[:, :]
                        if gain is not None and at_least(u, 1):
                            dve.wait_ge(done, u)
                        dve.tensor_tensor(out, cb[1 - j], rstd[:, 1 - j, :], ALU.mult).then_inc(normed_ready, 1)
                        if gain is not None:
                            dve.wait_ge(normed_ready, u + 1)
                            dve.tensor_scalar(part(dst, u), normed[:, :], gain, bias, ALU.mult, ALU.add).then_inc(done, 1)
            rounds(dve, 2, U // 2, 1, body)


def gated_ffn(nc, g, layer, last):
    W = 2 * T
    U = N // W
    NC = len(HCH)
    w1, b1, w2, b2 = g.l1_w1[layer], g.l1_b1[layer], g.l1_w2[layer], g.l1_b2[layer]
    with ExitStack() as ctx:
        g.n += 1

        def sb(name, shape, dt=F32):
            return ctx.enter_context(nc.sbuf_tensor(f"ff{g.n}_{name}", shape, dt))

        sems = []

        def sem(name):
            sems.append(ctx.enter_context(nc.semaphore(f"ff_{name}")))
            return sems[-1]
        gl = sb("gl", [P, NC, W])
        y = sb("y", [P, 2, NC, W])
        up_ready, gl_ready, y_ready, down_ready, z_ready, x_ready = (sem(x) for x in ("up_ready", "gl_ready", "y_ready", "down_ready", "z_ready", "x_ready"))
        ctx.callback(clear, nc, sems)
        block = ctx.enter_context(nc.Block())

        def part(x, s):
            return x[:, ds(s * W, W)] if not isinstance(s, int) else x[:, s * W:(s + 1) * W]

        @block.tensor
        def _(pe):
            def body(i):
                for j in range(2):
                    s = 2 * i + j
                    if runs(s, U):
                        for c, (c0, n) in enumerate(HCH):
                            if at_least(s, 1):
                                pe.wait_ge(y_ready, NC * (s - 1) + c + 1)
                            for half in range(2):
                                ins = nc.tensor.matmul(g.bank[2 * c + half][0:n], w1[:, half * HID + c0:half * HID + c0 + n], part(g.hn, s), start=True, stop=True)
                            ins.then_inc(up_ready, 1)
                    u = s - 1
                    if runs(u, U):
                        pe.wait_ge(y_ready, NC * (u + 1))
                        if at_least(u, 2):
                            pe.wait_ge(z_ready, u - 1)
                        for c, (c0, n) in enumerate(HCH):
                            ins = nc.tensor.matmul(g.bank[6 + (1 - j)], w2[0:n, c, :], y[0:n, 1 - j, c, :], start=(c == 0), stop=(c == NC - 1))
                        ins.then_inc(down_ready, 1)
            rounds(pe, 2, U // 2, 1, body)

        @block.scalar
        def _(act):
            def body(i):
                for j in range(2):
                    s = 2 * i + j
                    if runs(s, U):
                        for c, (c0, n) in enumerate(HCH):
                            act.wait_ge(up_ready, NC * s + c + 1)
                            act.activation(gl[0:n, c, :], g.bank[2 * c + 1][0:n], ACT.Gelu, bias=b1[0:n, NC + c:NC + c + 1]).then_inc(gl_ready, 1)
            rounds(act, 1, U // 2, 0, body)

        @block.vector
        def _(dve):
            def body(i):
                for j in range(2):
                    s = 2 * i + j
                    if runs(s, U):
                        for c, (c0, n) in enumerate(HCH):
                            dve.wait_ge(gl_ready, NC * s + c + 1)
                            if c == 0 and at_least(s, 2):
                                dve.wait_ge(down_ready, s - 1)
                            dve.scalar_tensor_tensor(y[0:n, j, c, :], g.bank[2 * c][0:n], b1[0:n, c:c + 1], gl[0:n, c, :], ALU.add, ALU.mult).then_inc(y_ready, 1)
                    u = s - 1
                    if runs(u, U):
                        dve.wait_ge(down_ready, u + 1)
                        dve.scalar_tensor_tensor(part(g.z, u), g.bank[6 + (1 - j)], b2, part(g.z, u), ALU.add, ALU.add).then_inc(z_ready, 1)
                        if last:
                            dve.wait_ge(z_ready, u + 1)
                            dve.scalar_tensor_tensor(part(g.x, u), part(g.z, u), 0.5, part(g.x, u), ALU.mult, ALU.add).then_inc(x_ready, 1)
            rounds(dve, 2, U // 2, 1, body)


def project_residual(nc, g, w, bias):
    W = 2 * T
    U = N // W
    with ExitStack() as ctx:
        g.n += 1
        sems = [ctx.enter_context(nc.semaphore(f"pj_{x}")) for x in ("out_ready", "x_ready")]
        out_ready, x_ready = sems
        ctx.callback(clear, nc, sems)
        block = ctx.enter_context(nc.Block())

        def part(x, s):
            return x[:, ds(s * W, W)] if not isinstance(s, int) else x[:, s * W:(s + 1) * W]

        @block.tensor
        def _(pe):
            def body(i):
                for j in range(2):
                    s = 2 * i + j
                    if at_least(s, 2):
                        pe.wait_ge(x_ready, s - 1)
                    nc.tensor.matmul(g.bank[j], w, part(g.hn, s), start=True, stop=True).then_inc(out_ready, 1)
            rounds(pe, 1, U // 2, 0, body)

        @block.vector
        def _(dve):
            def body(i):
                for j in range(2):
                    s = 2 * i + j
                    dve.wait_ge(out_ready, s + 1)
                    if bias is None:
                        dve.tensor_tensor(part(g.x, s), g.bank[j], part(g.x, s), ALU.add).then_inc(x_ready, 1)
                    else:
                        dve.scalar_tensor_tensor(part(g.x, s), g.bank[j], bias, part(g.x, s), ALU.add, ALU.add).then_inc(x_ready, 1)
            rounds(dve, 1, U // 2, 0, body)


SH, SD = 16, 8
EACH = 8
TRI = 384


def small_head_attention(nc, g, w, tab, qkv_bias, softmax):
    U = B * EACH
    qk_ps, rot_ps, v_ps, m1, m2, ol = g.bank[0], g.bank[1], g.bank[2], (g.bank[3], g.bank[4]), (g.bank[5], g.bank[6]), g.bank[7]
    pair1, pair2 = g.bank_pair3, g.bank_pair5
    mT = v_ps[0:4, T:T + P].bitcast(BF16)
    PV_LAG = 2
    S2_LAG = 1 if softmax else 0
    with ExitStack() as ctx:
        g.n += 1

        def sb(name, shape, dt=F32):
            return ctx.enter_context(nc.sbuf_tensor(f"sa{g.n}_{name}", shape, dt))

        sems = []

        def sem(name):
            sems.append(ctx.enter_context(nc.semaphore(f"sa_{name}")))
            return sems[-1]
        hT = sb("hT", [P, T])
        t1 = sb("t1", [P, 2 * T])
        t2 = sb("t2", [P, 2 * T])
        qk = sb("qk", [P, 2, 2 * T])
        km = sb("km", [P, 2, 4, T])
        vm = sb("vm", [P, 2, 2, 4 * (P + SD)])
        mx = sb("mx", [P, 2, 2])
        mp = sb("mp", [P, 2, 2, 2], BF16)
        mrow = sb("mrow", [P, T], BF16)
        pr = sb("pr", [P, 2, 2, TRI])
        rl = sb("rl", [P, T])
        o = sb("o", [P, T])
        names = ("h_ready", "v_zero", "proj_ready", "v_ready", "turned", "qk_ready", "km_ready", "s1_ready", "mx_done", "hi_done", "mx_ready",
                 "mT_ready", "mrow_ready", "s2_ready", "p_ready", "pv_ready", "ol_ready", "rl_done", "o_ready", "out_ready")
        (h_ready, v_zero, proj_ready, v_ready, turned, qk_ready, km_ready, s1_ready, mx_done, hi_done, mx_ready,
         mT_ready, mrow_ready, s2_ready, p_ready, pv_ready, ol_ready, rl_done, o_ready, out_ready) = (sem(x) for x in names)
        ctx.callback(clear, nc, sems)
        block = ctx.enter_context(nc.Block())
        mm = nc.tensor.matmul

        def tokens(x, b):
            return x[:, ds(b * T, T)] if not isinstance(b, int) else x[:, b * T:(b + 1) * T]

        def steps(i):
            for k in range(2):
                for e in range(EACH):
                    yield 2 * EACH * i + EACH * k + e, 2 * i + k, k, e

        def place(k, e, lag):
            n = (EACH * k + e - lag) % (2 * EACH)
            return n // EACH, n % EACH

        def heads(e):
            return (2 * (e % 2), 2 * (e % 2) + 1), e // 2

        @block.tensor
        def _(pe):
            def body(i):
                for s, b, k, e in steps(i):
                    u = s - 1
                    if softmax and runs(u, U):
                        kk, ee = place(k, e, 1)
                        pe.wait_ge(mx_ready, u + 1)
                        if at_least(u, 1):
                            pe.wait_ge(mrow_ready, u)
                        if isinstance(s, int) and s == 1:
                            pe.wait_ge(v_ready, 1)
                        if e == 5 and runs(b + 1, B):
                            pe.wait_ge(v_ready, b + 2)
                        for t in range(2):
                            ins = nc.tensor.transpose(mT[:, t * P:(t + 1) * P], mp[:, t, :, :].rearrange("p a h -> p (a h)"), g.ident[:, :])
                        ins.then_inc(mT_ready, 1)
                    if softmax and runs(s, U):
                        if e == 0:
                            pe.wait_ge(km_ready, b + 1)
                        if at_least(s, 1):
                            pe.wait_ge(mx_done, s)
                        gs, jj = heads(e)
                        for n, q in enumerate(gs):
                            r = slice(32 * q, 32 * q + 32)
                            mm(m1[n][:, 0:TRI], g.ident[:, :], g.tri_q[:, :], start=True, stop=False, skip_group_check=True)
                            mm(m1[n][:, 0:P], qk[r, k, 0:P], km[r, k, jj, 0:P], start=False, stop=False, skip_group_check=True)
                            ins = mm(m1[n][:, P:TRI], qk[r, k, P:T], km[r, k, jj, :], start=False, stop=True, skip_group_check=True)
                        ins.then_inc(s1_ready, 1)
                    u = s - PV_LAG
                    if runs(u, U):
                        kk, ee = place(k, e, PV_LAG)
                        gs, jj = heads(ee)
                        pe.wait_ge(p_ready, u + 1)
                        if ee == 0:
                            bb = b - 1 if e < PV_LAG else b
                            pe.wait_ge(v_ready, bb + 1)
                            if at_least(bb, 1):
                                pe.wait_ge(o_ready, bb)
                        for part in range(2 if softmax else 1):
                            for q0, col, n, kt in ((0, 0, T, 0), (P, T, P, 1)):
                                for m, q in enumerate(gs):
                                    cs = slice(32 * q, 32 * q + 32)
                                    wgt = vm[:, kk, kt, jj * P + 32 * q:jj * P + 32 * q + 32] if part == 0 else g.ones_j[:, jj, :]
                                    ins = mm(ol[cs, part * T + q0:part * T + q0 + n], wgt, pr[:, ee % 2, m, col:col + n],
                                             start=(jj == 0 and part == 0 and kt == 0), stop=(jj == 3 and kt == 1), skip_group_check=True)
                        ins.then_inc(pv_ready, 1)
                    u = s - S2_LAG
                    if runs(u, U):
                        kk, ee = place(k, e, S2_LAG)
                        gs, jj = heads(ee)
                        banks = m2 if softmax or ee % 2 else m1
                        if softmax:
                            pe.wait_ge(mrow_ready, u + 1)
                            if at_least(u, 1):
                                pe.wait_ge(p_ready, u)
                        else:
                            if ee == 0:
                                pe.wait_ge(km_ready, b + 1)
                            if at_least(u, 2):
                                pe.wait_ge(p_ready, u - 1)
                        for n, q in enumerate(gs):
                            r = slice(32 * q, 32 * q + 32)
                            if softmax:
                                mm(banks[n][:, 0:TRI], g.ident[:, :], g.tri_k[:, :], start=True, stop=False, skip_group_check=True)
                                mm(banks[n][:, 0:T], g.pick2_all[:, n, :], mrow[:, :], start=False, stop=False, skip_group_check=True)
                                mm(banks[n][:, T:TRI], g.pick2_all[:, n, :], mrow[:, P:T], start=False, stop=False, skip_group_check=True)
                            mm(banks[n][:, 0:T], km[r, kk, jj, 0:P], qk[r, kk, 0:T], start=not softmax, stop=False, skip_group_check=True)
                            ins = mm(banks[n][:, T:TRI], km[r, kk, jj, P:T], qk[r, kk, P:T], start=False, stop=True, skip_group_check=True)
                        ins.then_inc(s2_ready, 1)
                    nb = b + 1
                    if e == 4 and runs(nb, B):
                        project(nb, s)

            def project(b, s):
                pe.wait_ge(h_ready, b + 1)
                if at_least(b, 1):
                    pe.wait_ge(turned, b)
                    pe.wait_ge(v_ready, b)
                    if softmax:
                        pe.wait_ge(mrow_ready, s)
                for n in range(2):
                    mm(qk_ps[:, n * T:(n + 1) * T], w[:, n, :], hT[:, :], start=(n == 0), stop=(n == 1), skip_group_check=True)
                for n in range(2):
                    mm(rot_ps[:, n * T:(n + 1) * T], w[:, 3 + n, :], hT[:, :], start=(n == 0), stop=(n == 1), skip_group_check=True)
                for t in range(2):
                    ins = mm(v_ps[:, t * P:(t + 1) * P], hT[:, t * P:(t + 1) * P], w[:, 2, :], start=(t == 0), stop=(t == 1), skip_group_check=True)
                ins.then_inc(proj_ready, 1)
            project(0, 0)
            rounds(pe, 1, B // 2 - 1, 2, body)

        @block.gpsimd
        def _(pool):
            pool.memset(mrow[:, :], 0.0)
            pool.memset(vm[:, :, :, :], 0.0).then_inc(v_zero, 1)
            pool.wait_ge(v_zero, 1)

            def body(i):
                for k in range(2):
                    b = 2 * i + k
                    if at_least(b, 1):
                        pool.wait_ge(proj_ready, b)
                    pool.tensor_copy(hT[:, :], tokens(g.hn, b)).then_inc(h_ready, 1)
                    pool.wait_ge(turned, b + 1)
                    if at_least(b, 2):
                        pool.wait_ge(s2_ready, EACH * (b - 1))
                    pool.wait_ge(h_ready, b + 1)
                    pool.tensor_tensor(qk[:, k, :], t1[:, :], t2[:, :], ALU.add).then_inc(qk_ready, 1)
                    pool.wait_ge(qk_ready, b + 1)
            rounds(pool, 1, B // 2, 0, body)

        @block.scalar
        def _(act):
            if softmax:
                act.preload_act_table_set(LN_EXP)
            act.wait_ge(v_zero, 1)

            def values(b, k):
                act.wait_ge(proj_ready, b + 1)
                if at_least(b, 2):
                    act.wait_ge(pv_ready, EACH * (b - 1))
                for kt in range(2):
                    dst = vm[:, k, kt, :].rearrange("p (j x) -> p j x", j=4)[:, :, 0:P].rearrange("p j (g y) -> p j g y", g=4)[:, :, :, 0:SD]
                    src = v_ps[:, kt * P:(kt + 1) * P].rearrange("p (g j d) -> p j g d", g=4, j=4)
                    ins = act.activation(dst, src, ACT.Copy)
                ins.then_inc(v_ready, 1)

            def body(i):
                for s, b, k, e in steps(i):
                    u = s - 1
                    if softmax and runs(u, U):
                        kk, ee = place(k, e, 1)
                        act.wait_ge(mT_ready, u + 1)
                        if at_least(u, 1):
                            act.wait_ge(s2_ready, u)
                        act.activation(mrow[0:4, :], mT, ACT.Copy).then_inc(mrow_ready, 1)
                        act.wait_ge(s2_ready, u + 1)
                        if at_least(u, 2):
                            act.wait_ge(pv_ready, u - 1)
                        act.activation(pr[:, ee % 2, :, :], pair2[:, :, 0:TRI], ACT.Exp).then_inc(p_ready, 1)
                    if e == 4 and runs(b + 1, B):
                        values(b + 1, 1 - k)
                    if e == PV_LAG and runs(b - 1, B):
                        if softmax:
                            act.wait_ge(o_ready, b)
                            act.activation(tokens(g.hn, b - 1), o[:, :], ACT.Identity, bias=qkv_bias[:, 2:3]).then_inc(out_ready, 1)
                        else:
                            act.wait_ge(ol_last, EACH * b)
                            act.activation(tokens(g.hn, b - 1), ol[:, 0:T], ACT.Copy).then_inc(o_ready, 1)
            ol_last = pv_ready
            values(0, 0)
            rounds(act, 1, B // 2 - 1, 2, body)

        @block.vector
        def _(dve):
            def turn(b, k):
                dve.wait_ge(proj_ready, b + 1)
                if at_least(b, 1):
                    dve.wait_ge(qk_ready, b)
                for n in range(2):
                    cs = slice(n * T, (n + 1) * T)
                    if qkv_bias is None:
                        dve.tensor_tensor(t1[:, cs], qk_ps[:, cs], tab[:, 0, cs], ALU.mult)
                        ins = dve.tensor_tensor(t2[:, cs], rot_ps[:, cs], tab[:, 1, cs], ALU.mult)
                    else:
                        dve.scalar_tensor_tensor(t1[:, cs], qk_ps[:, cs], qkv_bias[:, n:n + 1], tab[:, 0, cs], ALU.add, ALU.mult)
                        ins = dve.scalar_tensor_tensor(t2[:, cs], rot_ps[:, cs], qkv_bias[:, 3 + n:4 + n], tab[:, 1, cs], ALU.add, ALU.mult)
                ins.then_inc(turned, 1)
                dve.wait_ge(qk_ready, b + 1)
                if at_least(b, 2):
                    dve.wait_ge(s2_ready, EACH * (b - 1))
                for jj in range(4):
                    ins = dve.tensor_scalar(km[:, k, jj, :], qk[:, k, T:2 * T], g.head_j[:, jj:jj + 1], None, ALU.mult)
                ins.then_inc(km_ready, 1)

            def body(i):
                for s, b, k, e in steps(i):
                    if softmax and runs(s, U):
                        dve.wait_ge(s1_ready, s + 1)
                        dve.reduce_max(mx[:, 0, :], pair1[:, :, 0:P], AX.X)
                        dve.reduce_max(mx[:, 1, :], pair1[:, :, P:TRI], AX.X).then_inc(mx_done, 1)
                        dve.wait_ge(mx_done, s + 1)
                        if at_least(s, 1):
                            dve.wait_ge(mT_ready, s)
                        dve.tensor_scalar(mp[:, :, 0, :], mx[:, :, :], -1.0, None, ALU.mult).then_inc(hi_done, 1)
                        dve.wait_ge(hi_done, s + 1)
                        dve.scalar_tensor_tensor(mp[:, :, 1, :], mx[:, :, :], -1.0, mp[:, :, 0, :], ALU.mult, ALU.subtract).then_inc(mx_ready, 1)
                    if not softmax and runs(s, U):
                        dve.wait_ge(s2_ready, s + 1)
                        if at_least(s, 2):
                            dve.wait_ge(pv_ready, s - 1)
                        src = (pair2 if e % 2 else pair1)[:, :, 0:TRI]
                        dve.tensor_tensor(pr[:, e % 2, :, :], src, g.tri_01[:, :].rearrange("p (h n) -> p h n", h=2), ALU.mult).then_inc(p_ready, 1)
                    if e == 4 and runs(b + 1, B):
                        turn(b + 1, 1 - k)
                    if softmax and e == PV_LAG and runs(b - 1, B):
                        dve.wait_ge(pv_ready, EACH * b)
                        dve.reciprocal(rl[:, :], ol[:, T:2 * T]).then_inc(rl_done, 1)
                        dve.wait_ge(rl_done, b)
                        if at_least(b, 2):
                            dve.wait_ge(out_ready, b - 1)
                        dve.tensor_tensor(o[:, :], ol[:, 0:T], rl[:, :], ALU.mult).then_inc(o_ready, 1)
            turn(0, 0)
            rounds(dve, 1, B // 2 - 1, 2, body)


EX, FH = 8, 512
TILES = N // P
BLOCKS = TILES + EX


def route(nc, g, turn):
    with ExitStack() as ctx:
        g.n += 1

        def sb(name, shape, dt=F32):
            return ctx.enter_context(nc.sbuf_tensor(f"ro{g.n}_{name}", shape, dt))

        sems = []

        def sem(name):
            sems.append(ctx.enter_context(nc.semaphore(f"ro_{name}")))
            return sems[-1]
        I32 = mybir.dt.int32
        logit = sb("logit", [P, TILES, EX])
        score = sb("score", [P, TILES, EX])
        onehot = sb("onehot", [P, TILES, EX])
        run = [sb(f"run{k}", [P, TILES, EX]) for k in range(2)]
        top = sb("top", [P, TILES])
        top2 = sb("top2", [P, TILES])
        full = sb("full", [P, EX])
        full_i = sb("full_i", [P, EX], I32)
        ends = [sb(f"ends{k}", [P, EX]) for k in range(2)]
        first = sb("first", [P, EX])
        total = sb("total", [P, TILES, EX])
        pos = sb("pos", [P, TILES])
        owner = sb("owner", [P, BLOCKS, EX])
        owned = sb("owned", [P, BLOCKS])
        xt = sb("xt", [P, TILES, P])
        logits_ready, onehot_ready, counts_ready, xt_ps, xt_ready, place_ready, step = (sem(x) for x in (
            "logits_ready", "onehot_ready", "counts_ready", "xt_ps", "xt_ready", "place_ready", "step"))
        ctx.callback(clear, nc, sems)
        block = ctx.enter_context(nc.Block())
        lg_ps = g.bank[0][:, 0:TILES * EX].rearrange("p (t e) -> p t e", e=EX)
        pre_ps = g.bank[1][:, 0:TILES * EX].rearrange("p (t e) -> p t e", e=EX)
        cnt_ps = g.bank[2][:, 0:TILES * EX].rearrange("p (t e) -> p t e", e=EX)

        @block.tensor
        def _(pe):
            for t in range(TILES):
                ins = nc.tensor.matmul(lg_ps[:, t, :], g.hn[:, t * P:(t + 1) * P], g.router_w, start=(t == 0), stop=(t == TILES - 1), skip_group_check=True)
            ins.then_inc(logits_ready, 1)

            def turn_tokens(q):
                if q >= 4:
                    pe.wait_ge(xt_ready, q - 3)
                for k in range(4):
                    t = 4 * q + k
                    ins = nc.tensor.transpose(g.bank[3 + q % 4][:, k * P:(k + 1) * P], g.hn[:, t * P:(t + 1) * P], g.ident32)
                ins.then_inc(xt_ps, 1)
            for q in range(4):
                turn_tokens(q)
            pe.wait_ge(onehot_ready, 1)
            nc.tensor.matmul(g.bank[1][:, 0:TILES * EX], g.before, onehot[:, :, :].rearrange("p t e -> p (t e)"), start=True, stop=True)
            nc.tensor.matmul(g.bank[2][:, 0:TILES * EX], g.ones, onehot[:, :, :].rearrange("p t e -> p (t e)"), start=True, stop=True).then_inc(counts_ready, 1)
            for q in range(4, TILES // 4):
                turn_tokens(q)

        @block.scalar
        def _(act):
            for q in range(TILES // 4):
                act.wait_ge(xt_ps, q + 1)
                act.activation(xt[:, 4 * q:4 * q + 4, :].rearrange("p t c -> p (t c)"), g.bank[3 + q % 4], ACT.Copy).then_inc(xt_ready, 1)

        @block.vector
        def _(dve):
            count = [0]

            def link(ins):
                count[0] += 1
                ins.then_inc(step, 1)
                dve.wait_ge(step, count[0])
            each = lambda x, n=TILES: x.unsqueeze(1).to_broadcast([P, n, EX])
            one = lambda x, n=TILES: x.unsqueeze(2).to_broadcast([P, n, EX])
            dve.wait_ge(logits_ready, 1)
            link(dve.tensor_tensor(logit[:, :, :], lg_ps, each(g.router_b), ALU.add))
            link(dve.reduce_max(top[:, :], logit[:, :, :], AX.X))
            link(dve.tensor_tensor(score[:, :, :], logit[:, :, :], one(top[:, :]), ALU.is_equal))
            link(dve.tensor_tensor(score[:, :, :], score[:, :, :], each(g.down8), ALU.mult))
            link(dve.reduce_max(top2[:, :], score[:, :, :], AX.X))
            dve.tensor_tensor(onehot[:, :, :], score[:, :, :], one(top2[:, :]), ALU.is_equal).then_inc(onehot_ready, 1)
            dve.wait_ge(counts_ready, 1)
            link(dve.tensor_copy(run[0][:, :, :], cnt_ps))
            cur = 0
            k = 1
            while k < TILES:
                dve.tensor_copy(run[1 - cur][:, 0:k, :], run[cur][:, 0:k, :])
                link(dve.tensor_tensor(run[1 - cur][:, k:, :], run[cur][:, k:, :], run[cur][:, 0:TILES - k, :], ALU.add))
                cur, k = 1 - cur, 2 * k
            inc = run[cur]
            link(dve.tensor_scalar(full[:, :], inc[:, TILES - 1, :], float(P - 1), None, ALU.add))
            link(dve.tensor_copy(full_i[:, :], full[:, :]))
            link(dve.tensor_scalar(full_i[:, :], full_i[:, :], 7, None, ALU.arith_shift_right))
            link(dve.tensor_copy(full[:, :], full_i[:, :]))
            link(dve.tensor_copy(ends[0][:, :], full[:, :]))
            e, k = 0, 1
            while k < EX:
                dve.tensor_copy(ends[1 - e][:, 0:k], ends[e][:, 0:k])
                link(dve.tensor_tensor(ends[1 - e][:, k:], ends[e][:, k:], ends[e][:, 0:EX - k], ALU.add))
                e, k = 1 - e, 2 * k
            end = ends[e]
            link(dve.tensor_tensor(first[:, :], end[:, :], full[:, :], ALU.subtract))
            link(dve.tensor_scalar(first[:, :], first[:, :], float(P), None, ALU.mult))
            link(dve.tensor_tensor(total[:, :, :], pre_ps, inc[:, :, :], ALU.add))
            link(dve.tensor_tensor(total[:, :, :], total[:, :, :], each(first[:, :]), ALU.add))
            link(dve.tensor_tensor(total[:, :, :], total[:, :, :], cnt_ps, ALU.subtract))
            link(dve.tensor_tensor(total[:, :, :], total[:, :, :], onehot[:, :, :], ALU.mult))
            link(dve.reduce_sum(pos[:, :], total[:, :, :], AX.X))
            dve.tensor_copy(g.place[:, :], pos[:, :])
            link(dve.tensor_tensor(owner[:, :, :], one(g.block_of, BLOCKS), each(end[:, :], BLOCKS), ALU.is_ge))
            link(dve.reduce_sum(owned[:, :], owner[:, :, :], AX.X))
            link(dve.tensor_scalar(owned[:, :], owned[:, :], float(EX - 1), None, ALU.min))
            dve.tensor_copy(g.block_expert[:, :], owned[:, :]).then_inc(place_ready, 1)

        @block.gpsimd
        def _(pool):
            pool.wait_ge(place_ready, 1)
            for t in range(TILES):
                pool.wait_ge(xt_ready, t // 4 + 1)
                pool.indirect_dma_start(out=g.sorted_x, out_offset=bass.IndirectOffsetOnAxis(ap=g.place[:, t:t + 1], axis=0),
                                        in_=xt[:, t, :], in_offset=None).then_inc(g.sent, 16)
            pool.wait_ge(g.sent, 16 * TILES * turn)


def experts(nc, g):
    KC, WC = P, FH // P
    with ExitStack() as ctx:
        g.n += 1

        def sb(name, shape, dt=F32):
            return ctx.enter_context(nc.sbuf_tensor(f"ex{g.n}_{name}", shape, dt))

        sems = []

        def sem(name):
            sems.append(ctx.enter_context(nc.semaphore(f"ex_{name}")))
            return sems[-1]
        xb = sb("xb", [P, 2, P])
        xT = sb("xT", [P, 2, P])
        w1 = sb("w1", [P, 2, 2 * FH])
        w2 = sb("w2", [P, 2, WC * P])
        b1 = sb("b1", [P, 2, 2 * WC])
        b2 = sb("b2", [P, 2, P])
        sg = sb("sg", [P, 2, WC, P])
        y = sb("y", [P, 2, WC, P])
        out = sb("out", [P, 2, P])
        xb_ready = [sem(f"xb_ready{k}") for k in range(2)]
        stored = [sem(f"stored{k}") for k in range(2)]
        names = ("xT_ps", "xT_ready", "w_part", "w_ready", "up_ready", "sg_ready", "y_ready", "down_ready", "out_ready")
        xT_ps, xT_ready, w_part, w_ready, up_ready, sg_ready, y_ready, down_ready, out_ready = (sem(x) for x in names)
        ctx.callback(clear, nc, sems)
        block = ctx.enter_context(nc.Block())

        def rows(x, s):
            return x[ds(s * P, P), :] if not isinstance(s, int) else x[s * P:(s + 1) * P, :]

        @block.sync
        def _(sp):
            def body(i):
                for k in range(2):
                    s = 2 * i + k
                    if runs(s, BLOCKS):
                        if at_least(s, 2):
                            sp.wait_ge(xT_ps, s - 1)
                        sp.dma_start(xb[:, k, :], rows(g.sorted_x, s)).then_inc(xb_ready[k], 16)
                    u = s - 4
                    if runs(u, BLOCKS):
                        sp.wait_ge(out_ready, u + 1)
                        sp.dma_start(rows(g.sorted_y, u), out[:, k, :]).then_inc(stored[k], 16)
            rounds(sp, 2, BLOCKS // 2, 2, body)
            for k in range(2):
                sp.wait_ge(stored[k], 16 * (BLOCKS // 2))

        @block.gpsimd
        def _(pool):
            def body(i):
                for k in range(2):
                    s = 2 * i + k
                    if at_least(s, 2):
                        pool.wait_ge(out_ready, s - 1)
                    e = pool.value_load(g.block_expert[0:1, ds(s, 1) if not isinstance(s, int) else slice(s, s + 1)], min_val=0, max_val=EX - 1)
                    pool.tensor_copy(w1[:, k, :], g.l0_w1[:, ds(e * (2 * FH), 2 * FH)])
                    pool.tensor_copy(w2[:, k, :], g.l0_w2[:, ds(e * (WC * P), WC * P)])
                    pool.tensor_copy(b1[:, k, :], g.l0_b1[:, ds(e * (2 * WC), 2 * WC)])
                    pool.tensor_copy(b2[:, k, :], g.l0_b2[:, ds(e * P, P)]).then_inc(w_ready, 1)
            rounds(pool, 1, BLOCKS // 2, 0, body)

        @block.tensor
        def _(pe):
            def body(i):
                for k in range(2):
                    s = 2 * i + k
                    if runs(s, BLOCKS):
                        pe.wait_ge(xb_ready[k], 16 * (i + 1))
                        if at_least(s, 2):
                            pe.wait_ge(xT_ready, s - 1)
                        nc.tensor.transpose(g.bank[k][:, 0:P], xb[:, k, :], g.ident32).then_inc(xT_ps, 1)
                    u, m = s - 1, 1 - k
                    if runs(u, BLOCKS):
                        pe.wait_ge(xT_ready, u + 1)
                        pe.wait_ge(w_ready, u + 1)
                        if at_least(u, 2):
                            pe.wait_ge(y_ready, u - 1)
                        for half in (1, 0):
                            for c in range(WC):
                                ins = nc.tensor.matmul(g.bank[2 + 2 * m + half][:, c * P:(c + 1) * P], w1[:, m, half * FH + c * P:half * FH + (c + 1) * P], xT[:, m, :],
                                                       start=(c == 0), stop=(c == WC - 1), skip_group_check=True)
                        ins.then_inc(up_ready, 1)
                    u, m = s - 2, k
                    if runs(u, BLOCKS):
                        pe.wait_ge(y_ready, u + 1)
                        if at_least(u, 2):
                            pe.wait_ge(out_ready, u - 1)
                        for c in range(WC):
                            ins = nc.tensor.matmul(g.bank[6 + m][:, 0:P], y[:, m, c, :], w2[:, m, c * P:(c + 1) * P], start=(c == 0), stop=(c == WC - 1))
                        ins.then_inc(down_ready, 1)
            rounds(pe, 2, BLOCKS // 2, 1, body)

        @block.scalar
        def _(act):
            def body(i):
                for k in range(2):
                    s = 2 * i + k
                    if runs(s, BLOCKS):
                        act.wait_ge(xT_ps, s + 1)
                        if at_least(s, 2):
                            act.wait_ge(up_ready, s - 1)
                        act.activation(xT[:, k, :], g.bank[k][:, 0:P], ACT.Copy).then_inc(xT_ready, 1)
                    u, m = s - 1, 1 - k
                    if runs(u, BLOCKS):
                        act.wait_ge(up_ready, u + 1)
                        if at_least(u, 2):
                            act.wait_ge(y_ready, u - 1)
                        for c in range(WC):
                            ins = act.activation(sg[:, m, c, :], g.bank[3 + 2 * m][:, c * P:(c + 1) * P], ACT.Sigmoid, bias=b1[:, m, WC + c:WC + c + 1])
                        ins.then_inc(sg_ready, 1)
            rounds(act, 2, BLOCKS // 2, 1, body)

        @block.vector
        def _(dve):
            def body(i):
                for k in range(2):
                    s = 2 * i + k
                    u, m = s - 1, 1 - k
                    if runs(u, BLOCKS):
                        dve.wait_ge(sg_ready, u + 1)
                        if at_least(u, 2):
                            dve.wait_ge(down_ready, u - 1)
                        for c in range(WC):
                            ins = dve.scalar_tensor_tensor(y[:, m, c, :], g.bank[2 + 2 * m][:, c * P:(c + 1) * P], b1[:, m, c:c + 1], sg[:, m, c, :], ALU.add, ALU.mult)
                        ins.then_inc(y_ready, 1)
                    u, m = s - 2, k
                    if runs(u, BLOCKS):
                        dve.wait_ge(down_ready, u + 1)
                        if at_least(u, 2):
                            dve.wait_ge(stored[m], 16 * (i - 1))
                        dve.tensor_tensor(out[:, m, :], g.bank[6 + m][:, 0:P], b2[:, m, :], ALU.add).then_inc(out_ready, 1)
            rounds(dve, 2, BLOCKS // 2, 1, body)


def collect(nc, g, turn):
    with ExitStack() as ctx:
        g.n += 1
        yt = ctx.enter_context(nc.sbuf_tensor(f"co{g.n}_yt", [P, TILES, P], F32))
        turned, x_ready = (ctx.enter_context(nc.semaphore(f"co_{x}")) for x in ("turned", "x_ready"))
        sems = [turned, x_ready]
        ctx.callback(clear, nc, sems)
        block = ctx.enter_context(nc.Block())

        @block.gpsimd
        def _(pool):
            for t in range(TILES):
                pool.indirect_dma_start(out=yt[:, t, :], out_offset=None, in_=g.sorted_y,
                                        in_offset=bass.IndirectOffsetOnAxis(ap=g.place[:, t:t + 1], axis=0)).then_inc(g.fetched[t // 4], 16)

        @block.tensor
        def _(pe):
            for q in range(TILES // 4):
                pe.wait_ge(g.fetched[q], 64 * turn)
                if q >= 2:
                    pe.wait_ge(x_ready, q - 1)
                for k in range(4):
                    ins = nc.tensor.transpose(g.bank[q % 2][:, k * P:(k + 1) * P], yt[:, 4 * q + k, :], g.ident32)
                ins.then_inc(turned, 1)

        @block.vector
        def _(dve):
            for q in range(TILES // 4):
                dve.wait_ge(turned, q + 1)
                x = g.x[:, q * 4 * P:(q + 1) * 4 * P]
                dve.scalar_tensor_tensor(x, g.bank[q % 2], 0.5, x, ALU.mult, ALU.add).then_inc(x_ready, 1)


WEIGHTS = dict(router_w=EX, router_b=EX, l0_w1=EX * 2 * FH, l0_w2=EX * FH, l0_b1=EX * 8, l0_b2=EX * P,
               l0_w=5 * P, l0_b=5, l0_wp=P, l0_bp=1, r1_w=5 * P, r1_wo=P, r1_gain=1, r1_bias=1,
               l1_w=2 * 5 * CH * P, l1_wo=2 * CH * P, l1_s=2 * 4, l1_gain=2, l1_bias=2, l1_w1=2 * 2 * HID, l1_b1=2 * 6, l1_w2=2 * 3 * P, l1_b2=2)


def split_columns(t, sizes):
    out, at = {}, 0
    for name, n in sizes.items():
        out[name] = t[:, at:at + n]
        at += n
    return out


def program(nc, x_in, weights_in, const_in, const16_in, x_out, phases=None):
    f, b = constants()
    f, b = ({k: v.shape[1] for k, v in c.items()} for c in (f, b))
    with ExitStack() as ctx:
        def sb(name, shape, dt=F32):
            return ctx.enter_context(nc.sbuf_tensor(name, shape, dt))
        cf, cb, wt = sb("cf", [P, sum(f.values())]), sb("cb", [P, sum(b.values())], BF16), sb("wt", [P, sum(WEIGHTS.values())])
        c32, c16, w = split_columns(cf, f), split_columns(cb, b), split_columns(wt, WEIGHTS)
        g = Shared()
        g.center = c32["center"]
        g.mean = c32["mean"]
        g.head64 = c32["head64"]
        g.ones = c32["ones"]
        g.tiny = c32["tiny"]
        g.l1_base = c32["l1_base"]
        g.l0_tab = c32["l0_tab"]
        g.r1_tab = c32["r1_tab"]
        g.head_j = c32["head_j"]
        g.ones_j = c32["ones_j"]
        g.head_center = c32["head_center"]
        g.head_mean = c32["head_mean"]
        g.before = c32["before"]
        g.ident32 = c32["ident32"]
        g.tri_01 = c32["tri_01"]
        g.down8 = c32["down8"]
        g.block_of = c32["block_of"]
        g.ident = c16["ident"]
        g.tri_k = c16["tri_k"]
        g.tri_q = c16["tri_q"]
        g.band_q = c16["band_q"]
        g.band_k = c16["band_k"]
        g.pick2 = c16["pick2"]
        g.router_w = w["router_w"]
        g.router_b = w["router_b"]
        g.l0_w1 = w["l0_w1"]
        g.l0_w2 = w["l0_w2"]
        g.l0_b1 = w["l0_b1"]
        g.l0_b2 = w["l0_b2"]
        g.l0_w = w["l0_w"]
        g.l0_b = w["l0_b"]
        g.l0_wp = w["l0_wp"]
        g.l0_bp = w["l0_bp"]
        g.r1_w = w["r1_w"]
        g.r1_wo = w["r1_wo"]
        g.r1_gain = w["r1_gain"]
        g.r1_bias = w["r1_bias"]
        g.l1_w = w["l1_w"]
        g.l1_wo = w["l1_wo"]
        g.l1_s = w["l1_s"]
        g.l1_gain = w["l1_gain"]
        g.l1_bias = w["l1_bias"]
        g.l1_w1 = w["l1_w1"]
        g.l1_b1 = w["l1_b1"]
        g.l1_w2 = w["l1_w2"]
        g.l1_b2 = w["l1_b2"]
        psum = ctx.enter_context(nc.psum_tensor("psum", [P, 8, 512], F32))
        g.bank = [psum[:, k, :] for k in range(8)]
        g.bank_pair3, g.bank_pair5 = psum[:, 3:5, :], psum[:, 5:7, :]
        g.x, g.z, g.hn = sb("x", [P, N]), sb("z", [P, N]), sb("hn", [P, N])
        g.place, g.block_expert = sb("place", [P, TILES], mybir.dt.uint32), sb("block_expert", [P, BLOCKS], mybir.dt.int32)
        tabs = sb("tabs", [P, 2, 2, 2, 2 * T // 2])
        g.pick2_all = g.pick2.rearrange("p (h k) -> p h k", h=2)
        g.pick2 = g.pick2[0:4].rearrange("p (h k) -> p h k", h=2)
        g.ones_j = g.ones_j.rearrange("p (j c) -> p j c", j=4)
        l0_tab, r1_tab, base = (x.rearrange("p (a n) -> p a n", a=2) for x in (g.l0_tab, g.r1_tab, g.l1_base))
        w5 = lambda x: x.rearrange("p (n c) -> p n c", n=5)
        g.l1_wqkv = [g.l1_w[:, l * 5 * CH * P:(l + 1) * 5 * CH * P].rearrange("p (n c k) -> p n c k", n=5, c=CH) for l in range(2)]
        g.l1_wo = [g.l1_wo[:, l * CH * P:(l + 1) * CH * P].rearrange("p (c k) -> p c k", c=CH) for l in range(2)]
        g.l1_tab = [tabs[:, l].rearrange("p a q n -> p a (q n)") for l in range(2)]
        g.l1_w1 = [g.l1_w1[:, l * 2 * HID:(l + 1) * 2 * HID] for l in range(2)]
        g.l1_b1 = [g.l1_b1[:, l * 6:(l + 1) * 6] for l in range(2)]
        g.l1_w2 = [g.l1_w2[:, l * 3 * P:(l + 1) * 3 * P].rearrange("p (c k) -> p c k", c=3) for l in range(2)]
        g.l1_b2 = [g.l1_b2[:, l:l + 1] for l in range(2)]
        g.sorted_x = nc.dram_tensor("sorted_x", (BLOCKS * P, P), F32, kind="Internal").ap()
        g.sorted_y = nc.dram_tensor("sorted_y", (BLOCKS * P, P), F32, kind="Internal").ap()

        loaded, zeroed, cleared, tabled = (ctx.enter_context(nc.semaphore(x)) for x in ("loaded", "zeroed", "cleared", "tabled"))
        with nc.Block() as block:
            @block.sync
            def _(sp):
                sp.dma_start(g.x[:, :], x_in).then_inc(loaded, 16)
                sp.dma_start(cf[:, :], const_in).then_inc(loaded, 16)
                sp.dma_start(cb[:, :], const16_in).then_inc(loaded, 16)
                sp.dma_start(wt[:, :], weights_in).then_inc(loaded, 16)
                sp.wait_ge(zeroed, 1)
                sp.dma_start(g.sorted_x.rearrange("(p n) c -> p (n c)", p=P)[:, 0:N], g.z[:, :]).then_inc(cleared, 16)
                sp.dma_start(g.sorted_x.rearrange("(p n) c -> p (n c)", p=P)[:, N:], g.z[:, 0:BLOCKS * P - N]).then_inc(cleared, 16)
                sp.wait_ge(loaded, 64)
                sp.wait_ge(cleared, 32)

            @block.vector
            def _(dve):
                dve.memset(g.z[:, :], 0.0).then_inc(zeroed, 1)
                dve.wait_ge(loaded, 64)
                for l in range(2):
                    for a in range(2):
                        for q in range(2):
                            n = l * 4 + a * 2 + q
                            ins = dve.tensor_scalar(tabs[:, l, a, q, :], base[:, a, q * T:(q + 1) * T], g.l1_s[:, n:n + 1], None, ALU.mult)
                ins.then_inc(tabled, 1)
                dve.wait_ge(tabled, 1)

        g.sent = ctx.enter_context(nc.semaphore("sent"))
        g.fetched = [ctx.enter_context(nc.semaphore(f"fetched{q}")) for q in range(TILES // 4)]
        g.moe_turns = 0

        def moe():
            g.moe_turns += 1
            layer_norm(nc, g, g.x, g.hn, g.center, g.mean)
            route(nc, g, g.moe_turns)
            experts(nc, g)
            collect(nc, g, g.moe_turns)

        def l0_attn():
            layer_norm(nc, g, g.x, g.hn, g.center, g.mean)
            small_head_attention(nc, g, w5(g.l0_w), l0_tab, g.l0_b, True)
            project_residual(nc, g, g.l0_wp, g.l0_bp)

        def l1_ffn():
            layer_norm(nc, g, g.x, g.z, g.center, g.mean)
            for l in range(2):
                local_attention(nc, g, l)
                layer_norm(nc, g, g.z, g.hn, g.center, g.mean, shift=True, gain=g.l1_gain[:, l:l + 1], bias=g.l1_bias[:, l:l + 1])
                gated_ffn(nc, g, l, l == 1)

        def l1_attn():
            layer_norm(nc, g, g.x, g.hn, g.center, g.mean)
            small_head_attention(nc, g, w5(g.r1_w), r1_tab, None, False)
            layer_norm(nc, g, g.hn, g.hn, g.head_center, g.head_mean, gain=g.r1_gain, bias=g.r1_bias)
            project_residual(nc, g, g.r1_wo, None)
        steps = [moe, l0_attn, moe, l1_ffn, l1_attn, l1_ffn]
        for k, stage in enumerate(steps):
            if phases is None or k in phases:
                stage()
        stored = ctx.enter_context(nc.semaphore("out_stored"))
        with nc.Block() as block:
            @block.sync
            def _(sp):
                sp.dma_start(x_out, g.x[:, :]).then_inc(stored, 16)
                sp.wait_ge(stored, 16)


def lay_out(x):
    a = {k: np.asarray(v) for k, v in x.items()}
    w = {}
    rows = lambda v: np.broadcast_to(np.asarray(v).reshape(1, -1), (P, np.asarray(v).size))
    cols = lambda v: np.ascontiguousarray(np.asarray(v).reshape(-1, P).T)
    w["router_w"], w["router_b"] = a["L0_ffn_router_w"], rows(a["L0_ffn_router_b"])
    w["l0_w1"] = a["L0_ffn_w1"].transpose(1, 0, 2)
    w["l0_w2"] = a["L0_ffn_w2"].reshape(EX, FH // P, P, P).transpose(2, 0, 1, 3)
    w["l0_b1"], w["l0_b2"] = cols(a["L0_ffn_b1"]), rows(a["L0_ffn_b2"])
    ch = np.arange(P)
    swap2 = ch ^ 1
    swap4 = ch ^ 4
    wa, ba = a["L0_attn_w_attn"], a["L0_attn_b_attn"]
    q, k, v = wa[:, 0:P], wa[:, P:2 * P], wa[:, 2 * P:]
    w["l0_w"] = np.stack([q, k, v, q[:, swap2], k[:, swap2]], 1)
    bq, bk, bv = ba[0:P], ba[P:2 * P], ba[2 * P:]
    w["l0_b"] = np.stack([bq, bk, bv, bq[swap2], bk[swap2]], 1)
    w["l0_wp"], w["l0_bp"] = a["L0_attn_w_proj"], a["L0_attn_b_proj"][:, None]
    q, k, v = a["L1_attn_Wq"].T, a["L1_attn_Wk"].T, a["L1_attn_Wv"].T
    w["r1_w"] = np.stack([q, k, v, q[:, swap4], k[:, swap4]], 1)
    w["r1_wo"] = a["L1_attn_Wo"].T
    w["r1_gain"], w["r1_bias"] = a["L1_attn_gn_weight"][:, None], a["L1_attn_gn_bias"][:, None]
    inner = LH * LD
    swap = np.arange(inner).reshape(-1, 2, LD // 2)[:, ::-1].reshape(-1)
    wl, ws = [], []
    for l in range(2):
        q, k, v = (a["L1_ffn_wqkv"][l][:, n * inner:(n + 1) * inner] for n in range(3))
        wl.append(np.stack([m.reshape(P, CH, P) for m in (q, k, v, q[:, swap], k[:, swap])], 1).reshape(P, -1))
        for order in (ch % LD, swap[ch] % LD):
            ws += [a["L1_ffn_q_scale"][l][order], a["L1_ffn_k_scale"][l][order]]
    w["l1_w"], w["l1_s"] = np.concatenate(wl, 1), np.stack(ws, 1)
    w["l1_wo"] = a["L1_ffn_wo"].reshape(2, CH, P, P).transpose(2, 0, 1, 3)
    w["l1_gain"], w["l1_bias"] = cols(a["L1_ffn_ln_g"]), cols(a["L1_ffn_ln_b"])
    w["l1_w1"] = a["L1_ffn_w1"].transpose(1, 0, 2)
    b1 = np.zeros((P, 2, 6), np.float32)
    w2 = np.zeros((P, 2, 3, P), np.float32)
    for l in range(2):
        for c, (c0, n) in enumerate(HCH):
            b1[:n, l, c] = a["L1_ffn_b1"][l][c0:c0 + n]
            b1[:n, l, 3 + c] = a["L1_ffn_b1"][l][HID + c0:HID + c0 + n]
            w2[:n, l, c] = a["L1_ffn_w2"][l][c0:c0 + n]
    w["l1_b1"], w["l1_w2"], w["l1_b2"] = b1, w2, cols(a["L1_ffn_b2"])
    weights = np.concatenate([w[k].reshape(P, -1) for k in WEIGHTS], 1)
    return np.ascontiguousarray(a["L0_attn_x"].reshape(N, P).T), np.ascontiguousarray(weights)


def kernel(**inputs):
    import concourse.bacc as bacc
    import ml_dtypes
    from concourse.bass_utils import run_bass_kernel_spmd

    nc = bacc.Bacc("TRN2", target_bir_lowering=False, num_devices=1)
    x, weights = lay_out(inputs)
    f, b = constants()
    arrays = {"x_t": x, "weights": weights, "const": np.concatenate(list(f.values()), 1),
              "const16": np.concatenate(list(b.values()), 1).astype(ml_dtypes.bfloat16)}
    args = [nc.dram_tensor(k, v.shape, mybir.dt.from_np(v.dtype), kind="ExternalInput").ap() for k, v in arrays.items()]
    out = nc.dram_tensor("x_final", (P, N), F32, kind="ExternalOutput").ap()
    program(nc, *args, out)
    got = run_bass_kernel_spmd(nc, [arrays], core_ids=[0]).results[0]["x_final"]
    return np.ascontiguousarray(np.asarray(got).T).reshape(B, T, P)
```
